# Optimizing a Trainium2 kernel written in Bass

```python
import numpy as np
import jax
import jax.numpy as jnp

def _softmax(x, axis=-1):
    return jax.nn.softmax(x, axis=axis)

def _gelu(x):
    return jax.nn.gelu(x, approximate=True)

def _silu(x):
    return jax.nn.silu(x)

def _sigmoid(x):
    return jax.nn.sigmoid(x)

def _layernorm(x, axis=-1, eps=1e-05):
    m = jnp.mean(x, axis=axis, keepdims=True)
    v = jnp.var(x, axis=axis, keepdims=True)
    return (x - m) / jnp.sqrt(v + eps)

def _scatter_add(tgt, idx, src, axis=0):
    return tgt.at[idx].add(src)

def _segment_sum(src, seg, n):
    return jax.ops.segment_sum(src, seg, n)
kernel_name = 'mk_adaln_ffn_d1_seqx_r4_63485c'

def setup_inputs(seed: int=0):
    np.random.seed(seed)
    _w = jnp.asarray

    def _rec_inputs():
        import jax
        import jax.numpy as jnp
        _rk = jax.random.key(seed)
        x = -7.109e-05 + 0.9999 * jax.random.normal(jax.random.fold_in(_rk, 1), (64, 64, 512), jnp.float32)
        _lenS = 64 - jax.random.randint(jax.random.fold_in(_rk, 7), (64,), 0, max(1, 64 // 4) + 1, jnp.int32)
        _lenS2 = 64 - jax.random.randint(jax.random.fold_in(_rk, 8), (64,), 0, max(1, 64 // 4) + 1, jnp.int32)
        itok_B_1_198 = jax.random.randint(jax.random.fold_in(_rk, 11), (64,), 1, 199, jnp.int32)
        return (x, itok_B_1_198)
    x, itok_B_1_198 = _rec_inputs()

    def _L0_cond_setup():
        import jax, jax.numpy as jnp
        import numpy as np
        B, C, T = (128, 64, 512)
        S, D = (200, 64)
        key = jax.random.key(seed)
        k1, k2, k3 = jax.random.split(key, 3)
        x = jax.random.normal(k1, (B, C, T), dtype=jnp.float32)
        conditions = jax.random.randint(k2, (B,), 0, S, dtype=jnp.int64)
        weights = jax.random.normal(k3, (S, C, D), dtype=jnp.float32) / jnp.sqrt(jnp.float32(C))
        return {'x': x, 'conditions': conditions, 'weights': weights}
    _L0_cond_all = _L0_cond_setup()
    _L0_cond_in = {k: v for k, v in _L0_cond_all.items() if k in ('weights',)}
    del _L0_cond_all

    def _L0_ffn_setup():
        import jax, jax.numpy as jnp
        import numpy as np
        TOP_K = 2
        key = jax.random.key(seed)
        ks = jax.random.split(key, 5)
        B, S, D, INTER, E = (4, 512, 512, 512, 8)
        x = jax.random.normal(ks[0], (B, S, D), dtype=jnp.float32)
        w1 = jax.random.normal(ks[1], (INTER, D), dtype=jnp.float32) * (1.0 / np.sqrt(D))
        w3 = jax.random.normal(ks[2], (INTER, INTER), dtype=jnp.float32) * (1.0 / np.sqrt(INTER))
        w2 = jax.random.normal(ks[3], (D, INTER), dtype=jnp.float32) * (1.0 / np.sqrt(INTER))
        wr = jax.random.normal(ks[4], (E, D), dtype=jnp.float32) * (1.0 / np.sqrt(D))
        return {'x': x, 'w1': w1, 'w3': w3, 'w2': w2, 'wr': wr}
    _L0_ffn_all = _L0_ffn_setup()
    _L0_ffn_in = {k: v for k, v in _L0_ffn_all.items() if k in ('w1', 'w3', 'w2', 'wr')}
    del _L0_ffn_all
    return {'x': x, 'itok_B_1_198': itok_B_1_198, 'L0_cond_weights': _L0_cond_in['weights'], 'L0_ffn_w1': _L0_ffn_in['w1'], 'L0_ffn_w3': _L0_ffn_in['w3'], 'L0_ffn_w2': _L0_ffn_in['w2'], 'L0_ffn_wr': _L0_ffn_in['wr']}

def reference(x, itok_B_1_198, L0_cond_weights, L0_ffn_w1, L0_ffn_w3, L0_ffn_w2, L0_ffn_wr):
    import jax
    import jax.numpy as jnp

    def _L0_cond_ref(x, conditions, weights):
        import jax, jax.numpy as jnp
        import numpy as np
        B, C, T = (128, 64, 512)
        S, D = (200, 64)
        w = weights[conditions]
        return jnp.einsum('bct,bcd->bdt', x, w)

    def _L0_ffn_ref(x, w1, w3, w2, wr):
        import jax, jax.numpy as jnp
        import numpy as np
        TOP_K = 2
        B, S, D = x.shape
        xr = x.reshape(-1, D)
        route_probs = jax.nn.softmax(xr @ wr.T, axis=-1)
        routes_k, indices_k = jax.lax.top_k(route_probs, TOP_K)
        gates = routes_k / jnp.sum(routes_k, axis=-1, keepdims=True)
        h = jax.nn.silu(xr @ w1.T)
        h = jax.nn.silu(h @ w3.T)
        h = h @ w2.T
        out = jnp.zeros_like(xr)
        for k in range(TOP_K):
            out = out.at[indices_k[:, k]].add(gates[:, k:k + 1] * h)
        return out.reshape(B, S, D)
    x = x + _L0_ffn_ref(_L0_cond_ref(x, itok_B_1_198, L0_cond_weights), L0_ffn_w1, L0_ffn_w3, L0_ffn_w2, L0_ffn_wr)
    return x

_drawn_inputs = setup_inputs


def setup_inputs(seed=0):
    import zlib

    import numpy as np

    out = dict(_drawn_inputs(seed))
    spreads = {}
    factors = {}
    for name, (base, spread) in spreads.items():
        noise = np.random.default_rng([zlib.crc32(name.encode()), seed]).standard_normal(out[name].shape)
        drawn = base * np.exp(spread * noise) if base else spread * noise
        out[name] = jnp.asarray(drawn.astype(out[name].dtype))
    for name, factor in factors.items():
        out[name] = (out[name] * factor).astype(out[name].dtype)
    return out
```

```python
from contextlib import ExitStack

import concourse.bass as bass
import numpy as np
from concourse import mybir

F32 = mybir.dt.float32
F32R = mybir.dt.float32r
I32 = mybir.dt.int32
ALU = mybir.AluOpType
ACT = mybir.ActivationFunctionType
AX_X = mybir.AxisListType.X

P = 128
QUAD = 32
FFN_BANKS = 3


def adaln_ffn(nc, x, cond, cond_w, w1T, w3T, w2T, wrT, sel, rank, out):
    B, C, T = x.shape
    NCOND, _, D = cond_w.shape
    E = rank.shape[1]
    KT = T // P
    BLK = 512
    NBLK = B * D // BLK
    NB = BLK // D
    NPAIR = NB // 2
    CH = BLK // P
    assert C == D == P // 2 and T == BLK and KT == CH == P // QUAD and B * D % BLK == 0

    x_blk = x.rearrange("b c t -> (b c) t").rearrange("(n j p) t -> n p j t", p=P, j=NPAIR)
    out_rows = out.rearrange("b c t -> (b c) t")
    out_blk = out_rows.rearrange("(n j p) t -> n p j t", p=P, j=NPAIR)

    with ExitStack() as ctx:
        def sb(name, shape, dt=F32):
            return ctx.enter_context(nc.sbuf_tensor(name, shape, dt))

        def sem(name):
            return ctx.enter_context(nc.semaphore(name))

        w1_raw, w3_raw, w2_raw = (sb(f"w{i}_raw", [P, KT, T]) for i in (1, 3, 2))
        w1_hi, w1_lo, w3_hi, w3_lo = (sb(n, [P, KT, T], F32R) for n in ("w1_hi", "w1_lo", "w3_hi", "w3_lo"))
        wr_sb = sb("wr_sb", [P, KT, QUAD])
        sel_sb = sb("sel_sb", [P, E])
        rank_sb = sb("rank_sb", [P, CH, E])
        cond_sb = sb("cond_sb", [1, B], I32)
        cond_neg = sb("cond_neg", [1, B], I32)
        cond_wrap = sb("cond_wrap", [1, B], I32)
        cond_idx = sb("cond_idx", [1, B], I32)
        x_sb = sb("x_sb", [P, NPAIR, T])
        wc_sb = sb("wc_sb", [P, NPAIR, P])
        y = sb("y", [P, KT, BLK])
        y_hi, y_lo = sb("y_hi", [P, KT, BLK], F32R), sb("y_lo", [P, KT, BLK], F32R)
        h1 = sb("h1", [P, KT, BLK])
        h1_hi, h1_lo = sb("h1_hi", [P, KT, BLK], F32R), sb("h1_lo", [P, KT, BLK], F32R)
        h2 = sb("h2", [P, CH, T])
        lpart = sb("lpart", [P, BLK])
        top = sb("top", [P, CH])
        shifted = sb("shifted", [P, CH, E])
        expd = sb("expd", [P, CH, E])
        denom = sb("denom", [P, CH])
        rdenom = sb("rdenom", [P, CH])
        prob = sb("prob", [P, CH, E])
        best1, best2, pick1, pick2 = (sb(n, [P, CH]) for n in ("best1", "best2", "pick1", "pick2"))
        cand1, cand2, hot1, hot2 = (sb(n, [P, CH, E]) for n in ("cand1", "cand2", "hot1", "hot2"))
        rest = sb("rest", [P, CH, E])
        both = sb("both", [P, CH, E])
        kept = sb("kept", [P, CH, E])
        gsum, rgsum = sb("gsum", [P, CH]), sb("rgsum", [P, CH])
        gates = sb("gates", [P, CH, QUAD])
        s_sb = sb("s_sb", [P, T])
        sT_sb = sb("sT_sb", [P, KT, E])
        x8 = sb("x8", [E, T])
        o8 = sb("o8", [E, T])

        def bank(name):
            return ctx.enter_context(nc.psum_tensor(name, [P, 512], F32))

        y_ps = [bank(f"y_ps{k}") for k in range(KT)]
        ffn_ps = [bank(f"ffn_ps{i}") for i in range(FFN_BANKS)]
        s_ps = bank("s_ps")
        lpart_ps = y_ps[0]
        logit_ps = y_ps[1][:, 0:CH * E].rearrange("p (c e) -> p c e", e=E)
        sT_ps = y_ps[2][:, 0:KT * E].rearrange("p (c e) -> p c e", e=E)
        o8_ps = y_ps[3]

        cond_loaded, cond_step, cond_ready = sem("cond_loaded"), sem("cond_step"), sem("cond_ready")
        x_loaded, wc_loaded = sem("x_loaded"), sem("wc_loaded")
        w1_loaded, w3_loaded = ([sem(f"{w}_loaded{k}") for k in range(KT)] for w in ("w1", "w3"))
        w2_loaded = sem("w2_loaded")
        consts_loaded, x8_loaded, stored = sem("consts_loaded"), sem("x8_loaded"), sem("stored")
        w1_hi_ready, w1_lo_ready = sem("w1_hi_ready"), sem("w1_lo_ready")
        w3_hi_ready, w3_lo_ready = sem("w3_hi_ready"), sem("w3_lo_ready")
        zeroed, wc_zeroed, s_zeroed = sem("zeroed"), sem("wc_zeroed"), sem("s_zeroed")
        y_done, y_copied = sem("y_done"), sem("y_copied")
        y_hi_ready, y_lo_ready = sem("y_hi_ready"), sem("y_lo_ready")
        ffn_done, ffn_read = sem("ffn_done"), sem("ffn_read")
        h1_hi_ready, h1_lo_ready = sem("h1_hi_ready"), sem("h1_lo_ready")
        lpart_done, lpart_copied, logits_done = sem("lpart_done"), sem("lpart_copied"), sem("logits_done")
        shifted_ready, exp_ready, gates_ready = sem("shifted_ready"), sem("exp_ready"), sem("gates_ready")
        routing_step, top_ready = sem("routing_step"), sem("top_ready")
        s_done, s_copied, sT_done, sT_copied = sem("s_done"), sem("s_copied"), sem("sT_done"), sem("sT_copied")
        o8_done, o8_ready = sem("o8_done"), sem("o8_ready")

        NFFN = KT + CH
        ROUTING_STEPS = 18
        back = [FFN_BANKS] * NFFN
        last_in = {i % FFN_BANKS: i for i in range(NFFN)}
        for i in range(FFN_BANKS):
            back[i] = i + NFFN - last_in[i]

        block = ctx.enter_context(nc.Block())

        @block.sync
        def _(sp):
            def load_x(n):
                sp.dma_start(x_sb[:], x_blk[n]).then_inc(x_loaded, 16)

            def load_wc(n):
                for i in range(NB):
                    j, h = i // 2, i % 2
                    c = sp.value_load(cond_idx[0:1, bass.ds(n * NB + i, 1)], min_val=0, max_val=NCOND - 1)
                    half = slice(h * C, (h + 1) * C)
                    sp.dma_start(wc_sb[half, j, half], cond_w[bass.ds(c, 1)].rearrange("a c d -> (a c) d")).then_inc(wc_loaded, 16)

            sp.dma_start(cond_sb[:], cond.rearrange("(a b) -> a b", a=1)).then_inc(cond_loaded, 16)
            load_x(0)
            sp.wait_ge(cond_ready, 1)
            sp.wait_ge(wc_zeroed, 1)
            load_wc(0)
            sp.wait_ge(x_loaded, 16)
            sp.dma_start(out_rows[E:P, :], x_sb[E:P, 0, :]).then_inc(stored, 16)
            sp.dma_start(out_blk[0, :, 1:, :], x_sb[:, 1:, :]).then_inc(stored, 16)
            with sp.Fori(1, NBLK) as n:
                sp.wait_ge(y_done, n * KT)
                sp.wait_ge(stored, n * 16 + 16)
                load_x(n)
                load_wc(n)
                sp.wait_ge(x_loaded, n * 16 + 16)
                sp.dma_start(out_blk[n], x_sb[:]).then_inc(stored, 16)
            sp.wait_ge(o8_ready, 1)
            sp.dma_start(out_rows[0:E, :], o8[:]).then_inc(stored, 16)
            sp.wait_ge(stored, 16 * (NBLK + 2))

        @block.scalar
        def _(act):
            w_of = lambda w: w.rearrange("(k p) f -> p k f", p=P)
            for k in range(KT):
                act.dma_start(w1_raw[:, k, :], w1T[k * P:(k + 1) * P, :]).then_inc(w1_loaded[k], 16)
            act.dma_start(wr_sb[:, :, 0:E], w_of(wrT)).then_inc(consts_loaded, 16)
            act.dma_start(sel_sb[:], sel).then_inc(consts_loaded, 16)
            act.dma_start(rank_sb[:], rank.rearrange("(a c) e -> a c e", a=1).to_broadcast([P, CH, E])
                          ).then_inc(consts_loaded, 16)
            for k in range(KT):
                act.dma_start(w3_raw[:, k, :], w3T[k * P:(k + 1) * P, :]).then_inc(w3_loaded[k], 16)
            act.dma_start(w2_raw[:], w_of(w2T)).then_inc(w2_loaded, 16)
            act.dma_start(x8[:], x.rearrange("b c t -> (b c) t")[0:E, :]).then_inc(x8_loaded, 16)

            def split_weight(raw, hi, loaded, ready):
                for k in range(KT):
                    act.wait_ge(loaded[k], 16)
                    nc.scalar.copy(hi[:, k, :], raw[:, k, :]).then_inc(ready, 1)

            def copy_y(n):
                for k in range(KT):
                    act.wait_ge(y_done, n * KT + k + 1)
                    nc.scalar.copy(y[:, k, :], y_ps[k][:]).then_inc(y_copied, 1)

            def silu_h1(n):
                for m in range(KT):
                    i = n * NFFN + m
                    act.wait_ge(ffn_done, i + 1)
                    nc.scalar.activation(h1[:, m, :], ffn_ps[m % FFN_BANKS][:], ACT.Silu).then_inc(ffn_read, 1)
                    act.wait_ge(ffn_read, i + 1)
                    nc.scalar.copy(h1_hi[:, m, :], h1[:, m, :]).then_inc(h1_hi_ready, 1)

            def silu_h2(n):
                for c in range(CH):
                    i = n * NFFN + KT + c
                    act.wait_ge(ffn_done, i + 1)
                    nc.scalar.activation(h2[:, c, :], ffn_ps[(KT + c) % FFN_BANKS][:], ACT.Silu
                                         ).then_inc(ffn_read, 1)

            def exp_logits(n):
                act.wait_ge(shifted_ready, n + 1)
                nc.scalar.activation(expd[:], shifted[:], ACT.Exp).then_inc(exp_ready, 1)

            def step(n, last=False):
                if not (isinstance(n, int) and n == 0):
                    act.wait_ge(h1_lo_ready, n * KT)
                silu_h1(n)
                if not last:
                    act.wait_ge(lpart_done, n + 1)
                    act.wait_ge(y_lo_ready, n * KT + KT)
                    copy_y(n + 1)
                exp_logits(n)
                if not (isinstance(n, int) and n == 0):
                    act.wait_ge(s_done, n)
                silu_h2(n)

            split_weight(w1_raw, w1_hi, w1_loaded, w1_hi_ready)
            copy_y(0)
            split_weight(w3_raw, w3_hi, w3_loaded, w3_hi_ready)
            act.wait_ge(s_zeroed, 1)
            step(0)
            with act.Fori(1, NBLK - 1) as n:
                step(n)
            step(NBLK - 1, last=True)

        @block.tensor
        def _(pe):
            def product_y(n):
                pe.wait_ge(x_loaded, n * 16 + 16)
                pe.wait_ge(wc_loaded, n * (16 * NB) + 16 * NB)
                for k in range(KT):
                    for j in range(NPAIR):
                        mm = nc.tensor.matmul(y_ps[k][:, j * P:(j + 1) * P], x_sb[:, j, k * P:(k + 1) * P],
                                              wc_sb[:, j, :], start=True, stop=True)
                    mm.then_inc(y_done, 1)

            def product_logits(n):
                pe.wait_ge(y_copied, n * KT + KT)
                for k in range(KT):
                    mm = nc.tensor.matmul(lpart_ps[k * QUAD:(k + 1) * QUAD, :], wr_sb[:, k, :], y[:, k, :],
                                          start=True, stop=True)
                mm.then_inc(lpart_done, 1)

            def turn_logits(n):
                pe.wait_ge(lpart_copied, n + 1)
                for c in range(CH):
                    mm = nc.tensor.matmul(logit_ps[:, c, :], lpart[:, c * P:(c + 1) * P], sel_sb[:],
                                          start=True, stop=True)
                mm.then_inc(logits_done, 1)

            def three_passes(bank_, lhs, rhs, k, first, last):
                (lhs_hi, lhs_lo), (rhs_hi, rhs_lo) = lhs, rhs
                nc.tensor.matmul(bank_[:], lhs_hi, rhs_hi, start=first, stop=False)
                nc.tensor.matmul(bank_[:], lhs_lo, rhs_hi, start=False, stop=False)
                return nc.tensor.matmul(bank_[:], lhs_hi, rhs_lo, start=False, stop=last)

            def bank_free(n, i):
                before = i - back[i]
                if isinstance(n, int) and n * NFFN + before < 0:
                    return
                pe.wait_ge(ffn_read, n * NFFN + before + 1)

            def product_h1(n):
                pe.wait_ge(y_hi_ready, n * KT + KT)
                pe.wait_ge(y_lo_ready, n * KT + KT)
                for m in range(KT):
                    bank_free(n, m)
                    for k in range(KT):
                        f = slice(m * P, (m + 1) * P)
                        mm = three_passes(ffn_ps[m % FFN_BANKS], (w1_hi[:, k, f], w1_lo[:, k, f]),
                                          (y_hi[:, k, :], y_lo[:, k, :]), k, k == 0, k == KT - 1)
                    mm.then_inc(ffn_done, 1)

            def product_h2(n, chunks):
                pe.wait_ge(h1_hi_ready, n * KT + KT)
                pe.wait_ge(h1_lo_ready, n * KT + KT)
                for c in chunks:
                    bank_free(n, KT + c)
                    for k in range(KT):
                        t = slice(c * P, (c + 1) * P)
                        mm = three_passes(ffn_ps[(KT + c) % FFN_BANKS], (h1_hi[:, k, t], h1_lo[:, k, t]),
                                          (w3_hi[:, k, :], w3_lo[:, k, :]), k, k == 0, k == KT - 1)
                    mm.then_inc(ffn_done, 1)

            def sum_tokens(n, stop=False):
                pe.wait_ge(gates_ready, n + 1)
                pe.wait_ge(ffn_read, n * NFFN + NFFN)
                for c in range(CH):
                    mm = nc.tensor.matmul(s_ps[c * QUAD:(c + 1) * QUAD, :], gates[:, c, :], h2[:, c, :],
                                          start=False, stop=stop, skip_group_check=True)
                mm.then_inc(s_done, 1)

            def step(n, first=False, last=False):
                product_h1(n)
                if not first:
                    sum_tokens(n - 1)
                if not last:
                    pe.wait_ge(shifted_ready, n + 1)
                    product_y(n + 1)
                if first:
                    pe.wait_ge(w3_hi_ready, KT)
                    pe.wait_ge(w3_lo_ready, KT)
                product_h2(n, range(CH // 2))
                if not last:
                    product_logits(n + 1)
                product_h2(n, range(CH // 2, CH))
                if not last:
                    turn_logits(n + 1)

            pe.wait_ge(zeroed, 3)
            for c in range(CH):
                mm = nc.tensor.matmul(s_ps[c * QUAD:(c + 1) * QUAD, :], gates[:, c, :], h2[:, c, :],
                                      start=True, stop=False, skip_group_check=True)
            mm.then_inc(s_zeroed, 1)
            product_y(0)
            pe.wait_ge(consts_loaded, 16 * 3)
            product_logits(0)
            turn_logits(0)
            pe.wait_ge(w1_hi_ready, KT)
            pe.wait_ge(w1_lo_ready, KT)
            step(0, first=True)
            with pe.Fori(1, NBLK - 1) as n:
                step(n)
            step(NBLK - 1, last=True)
            sum_tokens(NBLK - 1, stop=True)
            pe.wait_ge(s_copied, 1)
            for k in range(KT):
                mm = nc.tensor.matmul(sT_ps[:, k, :], s_sb[:, k * P:(k + 1) * P], sel_sb[:], start=True, stop=True)
            mm.then_inc(sT_done, 1)
            pe.wait_ge(w2_loaded, 16)
            pe.wait_ge(sT_copied, 1)
            for k in range(KT):
                mm = nc.tensor.matmul(o8_ps[0:E, :], sT_sb[:, k, :], w2_raw[:, k, :],
                                      start=(k == 0), stop=(k == KT - 1))
            mm.then_inc(o8_done, 1)

        @block.vector
        def _(dve):
            def spread(small):
                return small[:].unsqueeze(2).to_broadcast([P, CH, E])

            def clamp_cond():
                dve.wait_ge(cond_loaded, 16)
                nc.vector.tensor_scalar(cond_neg[:], cond_sb[:], 0, NCOND, ALU.is_lt, ALU.mult).then_inc(cond_step, 1)
                dve.wait_ge(cond_step, 1)
                nc.vector.tensor_tensor(cond_wrap[:], cond_sb[:], cond_neg[:], ALU.add).then_inc(cond_step, 1)
                dve.wait_ge(cond_step, 2)
                nc.vector.tensor_scalar(cond_idx[:], cond_wrap[:], 0, NCOND - 1, ALU.max, ALU.min
                                        ).then_inc(cond_ready, 1)

            def split_weight(raw, hi, lo, hi_ready, lo_ready):
                for k in range(KT):
                    dve.wait_ge(hi_ready, k + 1)
                    nc.vector.tensor_tensor(lo[:, k, :], raw[:, k, :], hi[:, k, :].bitcast(F32), ALU.subtract
                                            ).then_inc(lo_ready, 1)

            def split_y(n):
                for k in range(KT):
                    dve.wait_ge(y_copied, n * KT + k + 1)
                    nc.vector.tensor_copy(y_hi[:, k, :], y[:, k, :]).then_inc(y_hi_ready, 1)
                    dve.wait_ge(y_hi_ready, n * KT + k + 1)
                    nc.vector.tensor_tensor(y_lo[:, k, :], y[:, k, :], y_hi[:, k, :].bitcast(F32), ALU.subtract
                                            ).then_inc(y_lo_ready, 1)

            def split_h1(n):
                for m in range(KT):
                    dve.wait_ge(h1_hi_ready, n * KT + m + 1)
                    nc.vector.tensor_tensor(h1_lo[:, m, :], h1[:, m, :], h1_hi[:, m, :].bitcast(F32), ALU.subtract
                                            ).then_inc(h1_lo_ready, 1)

            def shift_logits(n):
                dve.wait_ge(lpart_done, n + 1)
                nc.vector.tensor_copy(lpart[:], lpart_ps[:]).then_inc(lpart_copied, 1)
                dve.wait_ge(logits_done, n + 1)
                nc.vector.tensor_reduce(top[:], logit_ps, AX_X, ALU.max).then_inc(top_ready, 1)
                dve.wait_ge(top_ready, n + 1)
                nc.vector.tensor_tensor(shifted[:], logit_ps, spread(top), ALU.subtract).then_inc(shifted_ready, 1)

            def make_gates(n):
                done = n * ROUTING_STEPS
                dve.wait_ge(exp_ready, n + 1)
                nc.vector.tensor_reduce(denom[:], expd[:], AX_X, ALU.add).then_inc(routing_step, 1)
                dve.wait_ge(routing_step, done + 1)
                nc.vector.reciprocal(rdenom[:], denom[:]).then_inc(routing_step, 1)
                dve.wait_ge(routing_step, done + 2)
                nc.vector.tensor_tensor(prob[:], expd[:], spread(rdenom), ALU.mult).then_inc(routing_step, 1)
                dve.wait_ge(routing_step, done + 3)
                nc.vector.tensor_reduce(best1[:], prob[:], AX_X, ALU.max).then_inc(routing_step, 1)
                dve.wait_ge(routing_step, done + 4)
                nc.vector.tensor_tensor(cand1[:], prob[:], spread(best1), ALU.is_ge).then_inc(routing_step, 1)
                dve.wait_ge(routing_step, done + 5)
                nc.vector.tensor_tensor(cand1[:], cand1[:], rank_sb[:], ALU.mult).then_inc(routing_step, 1)
                dve.wait_ge(routing_step, done + 6)
                nc.vector.tensor_reduce(pick1[:], cand1[:], AX_X, ALU.max).then_inc(routing_step, 1)
                dve.wait_ge(routing_step, done + 7)
                nc.vector.tensor_tensor(hot1[:], rank_sb[:], spread(pick1), ALU.is_equal).then_inc(routing_step, 1)
                dve.wait_ge(routing_step, done + 8)
                nc.vector.scalar_tensor_tensor(out=rest[:], in0=hot1[:], scalar=-2.0, in1=prob[:],
                                               op0=ALU.mult, op1=ALU.add).then_inc(routing_step, 1)
                dve.wait_ge(routing_step, done + 9)
                nc.vector.tensor_reduce(best2[:], rest[:], AX_X, ALU.max).then_inc(routing_step, 1)
                dve.wait_ge(routing_step, done + 10)
                nc.vector.tensor_tensor(cand2[:], rest[:], spread(best2), ALU.is_ge).then_inc(routing_step, 1)
                dve.wait_ge(routing_step, done + 11)
                nc.vector.tensor_tensor(cand2[:], cand2[:], rank_sb[:], ALU.mult).then_inc(routing_step, 1)
                nc.vector.tensor_tensor(gsum[:], best1[:], best2[:], ALU.add).then_inc(routing_step, 1)
                dve.wait_ge(routing_step, done + 13)
                nc.vector.tensor_reduce(pick2[:], cand2[:], AX_X, ALU.max).then_inc(routing_step, 1)
                nc.vector.reciprocal(rgsum[:], gsum[:]).then_inc(routing_step, 1)
                dve.wait_ge(routing_step, done + 15)
                nc.vector.tensor_tensor(hot2[:], rank_sb[:], spread(pick2), ALU.is_equal).then_inc(routing_step, 1)
                dve.wait_ge(routing_step, done + 16)
                nc.vector.tensor_tensor(both[:], hot1[:], hot2[:], ALU.add).then_inc(routing_step, 1)
                dve.wait_ge(routing_step, done + 17)
                nc.vector.tensor_tensor(kept[:], prob[:], both[:], ALU.mult).then_inc(routing_step, 1)
                dve.wait_ge(routing_step, done + 18)
                dve.wait_ge(s_done, n)
                nc.vector.tensor_tensor(gates[:, :, 0:E], kept[:], spread(rgsum), ALU.mult).then_inc(gates_ready, 1)

            def step(n, last=False):
                split_h1(n)
                if not last:
                    split_y(n + 1)
                make_gates(n)
                if not last:
                    shift_logits(n + 1)

            clamp_cond()
            nc.vector.memset(wc_sb[:], 0.0).then_inc(wc_zeroed, 1)
            nc.vector.memset(gates[:], 0.0).then_inc(zeroed, 1)
            nc.vector.memset(h2[:], 0.0).then_inc(zeroed, 1)
            nc.vector.memset(wr_sb[:, :, E:], 0.0).then_inc(zeroed, 1)
            split_weight(w1_raw, w1_hi, w1_lo, w1_hi_ready, w1_lo_ready)
            split_y(0)
            dve.wait_ge(consts_loaded, 16 * 3)
            shift_logits(0)
            split_weight(w3_raw, w3_hi, w3_lo, w3_hi_ready, w3_lo_ready)
            dve.wait_ge(s_zeroed, 1)
            step(0)
            with dve.Fori(1, NBLK - 1) as n:
                step(n)
            step(NBLK - 1, last=True)
            dve.wait_ge(s_done, NBLK)
            nc.vector.tensor_copy(s_sb[:], s_ps[:]).then_inc(s_copied, 1)
            dve.wait_ge(sT_done, 1)
            nc.vector.tensor_copy(sT_sb[:], sT_ps).then_inc(sT_copied, 1)
            dve.wait_ge(x8_loaded, 16)
            dve.wait_ge(o8_done, 1)
            nc.vector.tensor_tensor(o8[:], o8_ps[0:E, :], x8[:], ALU.add).then_inc(o8_ready, 1)


def kernel(x, itok_B_1_198, L0_cond_weights, L0_ffn_w1, L0_ffn_w3, L0_ffn_w2, L0_ffn_wr):
    import concourse.bacc as bacc
    from concourse.bass_utils import run_bass_kernel_spmd

    experts = L0_ffn_wr.shape[0]
    sel = np.zeros((P, experts), np.float32)
    for e in range(experts):
        sel[e::QUAD, e] = 1.0
    rank = np.tile(np.arange(experts, 0, -1, dtype=np.float32), (4, 1))
    arrays = {
        "x": np.ascontiguousarray(x),
        "cond": np.ascontiguousarray(itok_B_1_198),
        "cond_w": np.ascontiguousarray(L0_cond_weights),
        "w1T": np.ascontiguousarray(np.asarray(L0_ffn_w1).T),
        "w3T": np.ascontiguousarray(np.asarray(L0_ffn_w3).T),
        "w2T": np.ascontiguousarray(np.asarray(L0_ffn_w2).T),
        "wrT": np.ascontiguousarray(np.asarray(L0_ffn_wr).T),
        "sel": sel,
        "rank": rank,
    }
    nc = bacc.Bacc("TRN2", target_bir_lowering=False, num_devices=1)
    aps = {n: nc.dram_tensor(n, a.shape, mybir.dt.from_np(a.dtype), kind="ExternalInput").ap()
           for n, a in arrays.items()}
    out = nc.dram_tensor("out", x.shape, F32, kind="ExternalOutput").ap()
    adaln_ffn(nc, out=out, **aps)
    result = run_bass_kernel_spmd(nc, [arrays], core_ids=[0])
    return result.results[0]["out"]
```

```python
from contextlib import ExitStack

import concourse.bass as bass
import numpy as np
from concourse import mybir

F32 = mybir.dt.float32
F32R = mybir.dt.float32r
I32 = mybir.dt.int32
ALU = mybir.AluOpType
ACT = mybir.ActivationFunctionType
AX_X = mybir.AxisListType.X

P = 128
QUAD = 32
FFN_BANKS = 3


def adaln_ffn(nc, x, cond, cond_w, w1T, w3T, w2T, wrT, ident, rank, out):
    B, C, T = x.shape
    NCOND, _, D = cond_w.shape
    E = rank.shape[1]
    KT = T // P
    BLK = 512
    NBLK = B * D // BLK
    NB = BLK // D
    NPAIR = NB // 2
    CH = BLK // P
    assert C == D == P // 2 and T == BLK and KT == CH == P // QUAD and B * D % BLK == 0

    x_blk = x.rearrange("b c t -> (b c) t").rearrange("(n j p) t -> n p j t", p=P, j=NPAIR)
    out_rows = out.rearrange("b c t -> (b c) t")
    out_blk = out_rows.rearrange("(n j p) t -> n p j t", p=P, j=NPAIR)

    with ExitStack() as ctx:
        def sb(name, shape, dt=F32):
            return ctx.enter_context(nc.sbuf_tensor(name, shape, dt))

        def sem(name):
            return ctx.enter_context(nc.semaphore(name))

        w1_raw, w3_raw, w2_raw = (sb(f"w{i}_raw", [P, KT, T]) for i in (1, 3, 2))
        w1_hi, w1_lo, w3_hi, w3_lo = (sb(n, [P, KT, T], F32R) for n in ("w1_hi", "w1_lo", "w3_hi", "w3_lo"))
        wr_sb = sb("wr_sb", [P, KT, QUAD])
        ident_sb = sb("ident_sb", [P, P])
        rank_sb = sb("rank_sb", [P, CH, E])
        cond_sb = sb("cond_sb", [1, B], I32)
        cond_neg = sb("cond_neg", [1, B], I32)
        cond_wrap = sb("cond_wrap", [1, B], I32)
        cond_idx = sb("cond_idx", [1, B], I32)
        x_sb = sb("x_sb", [P, NPAIR, T])
        wc_sb = sb("wc_sb", [P, NPAIR, P])
        y = sb("y", [P, KT, BLK])
        y_hi, y_lo = sb("y_hi", [P, KT, BLK], F32R), sb("y_lo", [P, KT, BLK], F32R)
        h1 = sb("h1", [P, KT, BLK])
        h1_hi, h1_lo = sb("h1_hi", [P, KT, BLK], F32R), sb("h1_lo", [P, KT, BLK], F32R)
        h2 = sb("h2", [P, CH, T])
        lpart = sb("lpart", [P, BLK])
        logits = sb("logits", [P, CH, E])
        top = sb("top", [P, CH])
        shifted = sb("shifted", [P, CH, E])
        expd = sb("expd", [P, CH, E])
        denom = sb("denom", [P, CH])
        rdenom = sb("rdenom", [P, CH])
        prob = sb("prob", [P, CH, E])
        best1, best2, pick1, pick2 = (sb(n, [P, CH]) for n in ("best1", "best2", "pick1", "pick2"))
        cand1, cand2, hot1, hot2 = (sb(n, [P, CH, E]) for n in ("cand1", "cand2", "hot1", "hot2"))
        rest = sb("rest", [P, CH, E])
        both = sb("both", [P, CH, E])
        kept = sb("kept", [P, CH, E])
        gsum, rgsum = sb("gsum", [P, CH]), sb("rgsum", [P, CH])
        gates = sb("gates", [P, CH, QUAD])
        s_sb = sb("s_sb", [P, T])
        sT_sb = sb("sT_sb", [P, KT, QUAD])
        x8 = sb("x8", [P, P])
        o8 = sb("o8", [P, P])

        def bank(name):
            return ctx.enter_context(nc.psum_tensor(name, [P, 512], F32))

        y_ps = [bank(f"y_ps{k}") for k in range(KT)]
        ffn_ps = [bank(f"ffn_ps{i}") for i in range(FFN_BANKS)]
        s_ps = bank("s_ps")
        lpart_ps = y_ps[0]
        turned_ps = y_ps[1]
        sT_ps = y_ps[2]
        o8_ps = y_ps[3]

        def quadrants(bank_):
            return bank_[:].rearrange("p (c q r) -> p c r q", c=CH, q=CH)[:, :, 0:E, :]

        def first_rows(q):
            return slice(q * QUAD, q * QUAD + E)

        cond_loaded, cond_step, cond_ready = sem("cond_loaded"), sem("cond_step"), sem("cond_ready")
        x_loaded, wc_loaded = sem("x_loaded"), sem("wc_loaded")
        wc_first = [sem(f"wc_first{j}") for j in range(NPAIR)]
        w1_loaded = [sem(f"w1_loaded{k}") for k in range(KT)]
        w3_loaded, w2_loaded = sem("w3_loaded"), sem("w2_loaded")
        consts_loaded, stored = sem("consts_loaded"), sem("stored")
        x8_zeroed, x8_loaded = sem("x8_zeroed"), sem("x8_loaded")
        w1_hi_ready, w1_lo_ready = sem("w1_hi_ready"), sem("w1_lo_ready")
        w3_hi_ready, w3_lo_ready = sem("w3_hi_ready"), sem("w3_lo_ready")
        zeroed, wc_zeroed, s_zeroed = sem("zeroed"), sem("wc_zeroed"), sem("s_zeroed")
        y_done, y_copied = sem("y_done"), sem("y_copied")
        y_hi_ready, y_lo_ready = sem("y_hi_ready"), sem("y_lo_ready")
        ffn_done, ffn_read = sem("ffn_done"), sem("ffn_read")
        h1_hi_ready, h1_lo_ready = sem("h1_hi_ready"), sem("h1_lo_ready")
        lpart_done, lpart_copied, logits_done = sem("lpart_done"), sem("lpart_copied"), sem("logits_done")
        logits_ready = sem("logits_ready")
        shifted_ready, exp_ready, gates_ready = sem("shifted_ready"), sem("exp_ready"), sem("gates_ready")
        routing_step, top_ready = sem("routing_step"), sem("top_ready")
        s_done, s_copied, sT_done, sT_copied = sem("s_done"), sem("s_copied"), sem("sT_done"), sem("sT_copied")
        o8_done, o8_ready = sem("o8_done"), sem("o8_ready")

        NFFN = KT + CH
        ROUTING_STEPS = 18
        WARM_UP = 5
        back = [FFN_BANKS] * NFFN
        last_in = {i % FFN_BANKS: i for i in range(NFFN)}
        for i in range(FFN_BANKS):
            back[i] = i + NFFN - last_in[i]

        block = ctx.enter_context(nc.Block())

        def load_wc(eng, n, batches, loaded):
            for i in batches:
                j, h = i // 2, i % 2
                c = eng.value_load(cond_idx[0:1, bass.ds(n * NB + i, 1)], min_val=0, max_val=NCOND - 1)
                half = slice(h * C, (h + 1) * C)
                eng.dma_start(wc_sb[half, j, half], cond_w[bass.ds(c, 1)].rearrange("a c d -> (a c) d")
                              ).then_inc(loaded[j], 16)

        @block.sync
        def _(sp):
            sp.dma_start(cond_sb[:], cond.rearrange("(a b) -> a b", a=1)).then_inc(cond_loaded, 16)
            sp.dma_start(x_sb[:], x_blk[0]).then_inc(x_loaded, 16)
            sp.wait_ge(wc_zeroed, 1)
            sp.wait_ge(cond_ready, 1)
            load_wc(sp, 0, range(0, NB, 2), wc_first)
            sp.wait_ge(x_loaded, 16)
            for j in range(NPAIR):
                sp.wait_ge(wc_first[j], 2 * 16)
            sp.dma_start(out_rows[E:P, :], x_sb[E:P, 0, :]).then_inc(stored, 16)
            sp.dma_start(out_blk[0, :, 1:, :], x_sb[:, 1:, :]).then_inc(stored, 16)
            with sp.Fori(1, NBLK) as n:
                sp.wait_ge(y_done, n * KT)
                load_wc(sp, n, range(NB // 2), [wc_loaded] * NPAIR)
                sp.wait_ge(stored, n * 16 + 16)
                sp.dma_start(x_sb[:], x_blk[n]).then_inc(x_loaded, 16)
                load_wc(sp, n, range(NB // 2, NB), [wc_loaded] * NPAIR)
                sp.wait_ge(x_loaded, n * 16 + 16)
                sp.dma_start(out_blk[n], x_sb[:]).then_inc(stored, 16)
            sp.wait_ge(o8_ready, 1)
            for q in range(0, KT, 2):
                sp.dma_start(out_rows[0:E, q * P:(q + 1) * P], o8[first_rows(q), :]).then_inc(stored, 16)
            sp.wait_ge(stored, 16 * (NBLK + 1 + KT))

        @block.gpsimd
        def _(pool):
            pool.dma_start(wr_sb[:, :, 0:E], wrT.rearrange("(k p) e -> p k e", p=P)).then_inc(consts_loaded, 16)
            pool.dma_start(ident_sb[:], ident).then_inc(consts_loaded, 16)
            pool.dma_start(rank_sb[:], rank.rearrange("(a c) e -> a c e", a=1).to_broadcast([P, CH, E])
                           ).then_inc(consts_loaded, 16)
            for k in range(2, KT):
                pool.dma_start(w1_raw[:, k, :], w1T[k * P:(k + 1) * P, :]).then_inc(w1_loaded[k], 16)
            for j in range(NPAIR):
                pool.wait_ge(wc_first[j], 2 * 16)
            pool.dma_start(w3_raw[:], w3T.rearrange("(k p) f -> p k f", p=P)).then_inc(w3_loaded, 16)
            pool.wait_ge(y_done, 2 * KT)
            pool.dma_start(w2_raw[:], w2T.rearrange("(k p) f -> p k f", p=P)).then_inc(w2_loaded, 16)
            pool.wait_ge(x8_zeroed, 1)
            for q in range(KT):
                pool.dma_start(x8[first_rows(q), :], x.rearrange("b c t -> (b c) t")[0:E, q * P:(q + 1) * P]
                               ).then_inc(x8_loaded, 16)

        @block.scalar
        def _(act):
            def copy_y(n):
                for k in range(KT):
                    act.wait_ge(y_done, n * KT + k + 1)
                    nc.scalar.copy(y[:, k, :], y_ps[k][:]).then_inc(y_copied, 1)

            def silu_h1(n):
                for m in range(KT):
                    i = n * NFFN + m
                    act.wait_ge(ffn_done, i + 1)
                    nc.scalar.activation(h1[:, m, :], ffn_ps[m % FFN_BANKS][:], ACT.Silu).then_inc(ffn_read, 1)
                    act.wait_ge(ffn_read, i + 1)
                    nc.scalar.copy(h1_hi[:, m, :], h1[:, m, :]).then_inc(h1_hi_ready, 1)

            def silu_h2(n):
                for c in range(CH):
                    i = n * NFFN + KT + c
                    act.wait_ge(ffn_done, i + 1)
                    nc.scalar.activation(h2[:, c, :], ffn_ps[(KT + c) % FFN_BANKS][:], ACT.Silu
                                         ).then_inc(ffn_read, 1)

            def exp_logits(n):
                act.wait_ge(shifted_ready, n + 1)
                nc.scalar.activation(expd[:], shifted[:], ACT.Exp).then_inc(exp_ready, 1)

            def step(n, last=False):
                if not (isinstance(n, int) and n == 0):
                    act.wait_ge(h1_lo_ready, n * KT)
                silu_h1(n)
                if not last:
                    act.wait_ge(lpart_done, n + 1)
                    act.wait_ge(y_lo_ready, n * KT + KT)
                    copy_y(n + 1)
                exp_logits(n)
                if not (isinstance(n, int) and n == 0):
                    act.wait_ge(s_done, n)
                silu_h2(n)

            for k in range(2):
                act.dma_start(w1_raw[:, k, :], w1T[k * P:(k + 1) * P, :]).then_inc(w1_loaded[k], 16)
            act.wait_ge(wc_zeroed, 1)
            act.wait_ge(cond_ready, 1)
            load_wc(act, 0, range(1, NB, 2), wc_first)
            copy_y(0)
            act.wait_ge(s_zeroed, 1)
            step(0)
            with act.Fori(1, NBLK - 1) as n:
                step(n)
            step(NBLK - 1, last=True)
            act.wait_ge(o8_ready, 1)
            for q in range(1, KT, 2):
                act.dma_start(out_rows[0:E, q * P:(q + 1) * P], o8[first_rows(q), :]).then_inc(stored, 16)

        @block.tensor
        def _(pe):
            def product_y(n):
                pe.wait_ge(x_loaded, n * 16 + 16)
                pe.wait_ge(wc_loaded, n * (16 * NB))
                for k in range(KT):
                    for j in range(NPAIR):
                        mm = nc.tensor.matmul(y_ps[k][:, j * P:(j + 1) * P], x_sb[:, j, k * P:(k + 1) * P],
                                              wc_sb[:, j, :], start=True, stop=True)
                    mm.then_inc(y_done, 1)

            def product_first_y():
                pe.wait_ge(x_loaded, 16)
                for j in range(NPAIR):
                    pe.wait_ge(wc_first[j], 2 * 16)
                    for k in range(KT):
                        mm = nc.tensor.matmul(y_ps[k][:, j * P:(j + 1) * P], x_sb[:, j, k * P:(k + 1) * P],
                                              wc_sb[:, j, :], start=True, stop=True)
                        if j == NPAIR - 1:
                            mm.then_inc(y_done, 1)

            def product_logits(n):
                pe.wait_ge(y_copied, n * KT + KT)
                for k in range(KT):
                    mm = nc.tensor.matmul(lpart_ps[k * QUAD:(k + 1) * QUAD, :], wr_sb[:, k, :], y[:, k, :],
                                          start=True, stop=True)
                mm.then_inc(lpart_done, 1)

            def turn_logits(n):
                pe.wait_ge(lpart_copied, n + 1)
                for c in range(CH):
                    mm = nc.tensor.transpose(turned_ps[:, c * P:(c + 1) * P], lpart[:, c * P:(c + 1) * P], ident_sb[:])
                mm.then_inc(logits_done, 1)

            def three_passes(bank_, lhs, rhs, first, last):
                (lhs_hi, lhs_lo), (rhs_hi, rhs_lo) = lhs, rhs
                nc.tensor.matmul(bank_[:], lhs_hi, rhs_hi, start=first, stop=False)
                nc.tensor.matmul(bank_[:], lhs_lo, rhs_hi, start=False, stop=False)
                return nc.tensor.matmul(bank_[:], lhs_hi, rhs_lo, start=False, stop=last)

            def bank_free(n, i):
                before = i - back[i]
                if isinstance(n, int) and n * NFFN + before < 0:
                    return
                pe.wait_ge(ffn_read, n * NFFN + before + 1)

            def product_h1_head(n, first=False):
                for m in range(2):
                    bank_free(n, m)
                    f = slice(m * P, (m + 1) * P)
                    for k in range(KT):
                        if m == 0:
                            pe.wait_ge(y_hi_ready, n * KT + k + 1)
                            if first:
                                pe.wait_ge(w1_hi_ready, k + 1)
                                pe.wait_ge(w1_lo_ready, k + 1)
                        nc.tensor.matmul(ffn_ps[m][:], w1_hi[:, k, f], y_hi[:, k, :], start=(k == 0), stop=False)
                        nc.tensor.matmul(ffn_ps[m][:], w1_lo[:, k, f], y_hi[:, k, :], start=False, stop=False)
                for m in range(2):
                    f = slice(m * P, (m + 1) * P)
                    for k in range(KT):
                        if m == 0:
                            pe.wait_ge(y_lo_ready, n * KT + k + 1)
                        mm = nc.tensor.matmul(ffn_ps[m][:], w1_hi[:, k, f], y_lo[:, k, :],
                                              start=False, stop=(k == KT - 1))
                    mm.then_inc(ffn_done, 1)

            def product_h1(n, chunks):
                for m in chunks:
                    bank_free(n, m)
                    f = slice(m * P, (m + 1) * P)
                    for k in range(KT):
                        mm = three_passes(ffn_ps[m % FFN_BANKS], (w1_hi[:, k, f], w1_lo[:, k, f]),
                                          (y_hi[:, k, :], y_lo[:, k, :]), k == 0, k == KT - 1)
                    mm.then_inc(ffn_done, 1)

            def product_h2(n, chunks):
                for c in chunks:
                    bank_free(n, KT + c)
                    for k in range(KT):
                        if c == 0:
                            pe.wait_ge(h1_hi_ready, n * KT + k + 1)
                            pe.wait_ge(h1_lo_ready, n * KT + k + 1)
                        t = slice(c * P, (c + 1) * P)
                        mm = three_passes(ffn_ps[(KT + c) % FFN_BANKS], (h1_hi[:, k, t], h1_lo[:, k, t]),
                                          (w3_hi[:, k, :], w3_lo[:, k, :]), k == 0, k == KT - 1)
                    mm.then_inc(ffn_done, 1)

            def sum_tokens(n, stop=False):
                pe.wait_ge(gates_ready, n + 1)
                pe.wait_ge(ffn_read, n * NFFN + NFFN)
                for c in range(CH):
                    mm = nc.tensor.matmul(s_ps[c * QUAD:(c + 1) * QUAD, :], gates[:, c, :], h2[:, c, :],
                                          start=False, stop=stop, skip_group_check=True)
                mm.then_inc(s_done, 1)

            def step(n, first=False, last=False):
                if first:
                    product_h1_head(n, first=True)
                    pe.wait_ge(consts_loaded, 16 * 3)
                    product_logits(n)
                    product_h1(n, range(2, 3))
                    turn_logits(n)
                    product_h1(n, range(3, KT))
                else:
                    product_h1_head(n)
                    product_h1(n, range(2, KT))
                    sum_tokens(n - 1)
                if not last:
                    pe.wait_ge(shifted_ready, n + 1)
                    product_y(n + 1)
                if first:
                    pe.wait_ge(w3_hi_ready, KT)
                    pe.wait_ge(w3_lo_ready, KT)
                product_h2(n, range(CH // 2))
                if not last:
                    product_logits(n + 1)
                product_h2(n, range(CH // 2, CH))
                if not last:
                    turn_logits(n + 1)

            pe.wait_ge(zeroed, 3)
            for _i in range(WARM_UP):
                mm = nc.tensor.matmul(s_ps[:], gates[:].rearrange("p c e -> p (c e)"), h2[:, 0, :],
                                      start=True, stop=False, skip_group_check=True)
            mm.then_inc(s_zeroed, 1)
            product_first_y()
            step(0, first=True)
            with pe.Fori(1, NBLK - 1) as n:
                step(n)
            step(NBLK - 1, last=True)
            sum_tokens(NBLK - 1, stop=True)
            for k in range(KT):
                pe.wait_ge(s_copied, k + 1)
                mm = nc.tensor.transpose(sT_ps[:, k * P:(k + 1) * P], s_sb[:, k * P:(k + 1) * P], ident_sb[:])
            mm.then_inc(sT_done, 1)
            pe.wait_ge(w2_loaded, 16)
            pe.wait_ge(sT_copied, 1)
            for k in range(KT):
                for q in range(KT):
                    mm = nc.tensor.matmul(o8_ps[q * QUAD:(q + 1) * QUAD, 0:P], sT_sb[:, k, :],
                                          w2_raw[:, k, q * P:(q + 1) * P], start=(k == 0), stop=(k == KT - 1))
            mm.then_inc(o8_done, 1)

        @block.vector
        def _(dve):
            def spread(small):
                return small[:].unsqueeze(2).to_broadcast([P, CH, E])

            def clamp_cond():
                dve.wait_ge(cond_loaded, 16)
                nc.vector.tensor_scalar(cond_neg[:], cond_sb[:], 0, NCOND, ALU.is_lt, ALU.mult).then_inc(cond_step, 1)
                dve.wait_ge(cond_step, 1)
                nc.vector.tensor_tensor(cond_wrap[:], cond_sb[:], cond_neg[:], ALU.add).then_inc(cond_step, 1)
                dve.wait_ge(cond_step, 2)
                nc.vector.tensor_scalar(cond_idx[:], cond_wrap[:], 0, NCOND - 1, ALU.max, ALU.min
                                        ).then_inc(cond_ready, 1)

            def split_w1():
                for k in range(KT):
                    dve.wait_ge(w1_loaded[k], 16)
                    nc.vector.tensor_copy(w1_hi[:, k, :], w1_raw[:, k, :]).then_inc(w1_hi_ready, 1)
                    dve.wait_ge(w1_hi_ready, k + 1)
                    nc.vector.tensor_tensor(w1_lo[:, k, :], w1_raw[:, k, :], w1_hi[:, k, :].bitcast(F32), ALU.subtract
                                            ).then_inc(w1_lo_ready, 1)

            def split_w3():
                dve.wait_ge(w3_loaded, 16)
                for k in range(KT):
                    nc.vector.tensor_copy(w3_hi[:, k, :], w3_raw[:, k, :]).then_inc(w3_hi_ready, 1)
                    dve.wait_ge(w3_hi_ready, k + 1)
                    nc.vector.tensor_tensor(w3_lo[:, k, :], w3_raw[:, k, :], w3_hi[:, k, :].bitcast(F32), ALU.subtract
                                            ).then_inc(w3_lo_ready, 1)

            def split_y(n):
                for k in range(KT):
                    dve.wait_ge(y_copied, n * KT + k + 1)
                    nc.vector.tensor_copy(y_hi[:, k, :], y[:, k, :]).then_inc(y_hi_ready, 1)
                for k in range(KT):
                    dve.wait_ge(y_hi_ready, n * KT + k + 1)
                    nc.vector.tensor_tensor(y_lo[:, k, :], y[:, k, :], y_hi[:, k, :].bitcast(F32), ALU.subtract
                                            ).then_inc(y_lo_ready, 1)

            def split_h1(n):
                for m in range(KT):
                    dve.wait_ge(h1_hi_ready, n * KT + m + 1)
                    nc.vector.tensor_tensor(h1_lo[:, m, :], h1[:, m, :], h1_hi[:, m, :].bitcast(F32), ALU.subtract
                                            ).then_inc(h1_lo_ready, 1)

            def shift_logits(n):
                dve.wait_ge(lpart_done, n + 1)
                nc.vector.tensor_copy(lpart[:], lpart_ps[:]).then_inc(lpart_copied, 1)
                dve.wait_ge(logits_done, n + 1)
                nc.vector.tensor_reduce(logits[:], quadrants(turned_ps), AX_X, ALU.add).then_inc(logits_ready, 1)
                dve.wait_ge(logits_ready, n + 1)
                nc.vector.tensor_reduce(top[:], logits[:], AX_X, ALU.max).then_inc(top_ready, 1)
                dve.wait_ge(top_ready, n + 1)
                nc.vector.tensor_tensor(shifted[:], logits[:], spread(top), ALU.subtract).then_inc(shifted_ready, 1)

            def make_gates(n):
                done = n * ROUTING_STEPS
                dve.wait_ge(exp_ready, n + 1)
                nc.vector.tensor_reduce(denom[:], expd[:], AX_X, ALU.add).then_inc(routing_step, 1)
                dve.wait_ge(routing_step, done + 1)
                nc.vector.reciprocal(rdenom[:], denom[:]).then_inc(routing_step, 1)
                dve.wait_ge(routing_step, done + 2)
                nc.vector.tensor_tensor(prob[:], expd[:], spread(rdenom), ALU.mult).then_inc(routing_step, 1)
                dve.wait_ge(routing_step, done + 3)
                nc.vector.tensor_reduce(best1[:], prob[:], AX_X, ALU.max).then_inc(routing_step, 1)
                dve.wait_ge(routing_step, done + 4)
                nc.vector.tensor_tensor(cand1[:], prob[:], spread(best1), ALU.is_ge).then_inc(routing_step, 1)
                dve.wait_ge(routing_step, done + 5)
                nc.vector.tensor_tensor(cand1[:], cand1[:], rank_sb[:], ALU.mult).then_inc(routing_step, 1)
                dve.wait_ge(routing_step, done + 6)
                nc.vector.tensor_reduce(pick1[:], cand1[:], AX_X, ALU.max).then_inc(routing_step, 1)
                dve.wait_ge(routing_step, done + 7)
                nc.vector.tensor_tensor(hot1[:], rank_sb[:], spread(pick1), ALU.is_equal).then_inc(routing_step, 1)
                dve.wait_ge(routing_step, done + 8)
                nc.vector.scalar_tensor_tensor(out=rest[:], in0=hot1[:], scalar=-2.0, in1=prob[:],
                                               op0=ALU.mult, op1=ALU.add).then_inc(routing_step, 1)
                dve.wait_ge(routing_step, done + 9)
                nc.vector.tensor_reduce(best2[:], rest[:], AX_X, ALU.max).then_inc(routing_step, 1)
                dve.wait_ge(routing_step, done + 10)
                nc.vector.tensor_tensor(cand2[:], rest[:], spread(best2), ALU.is_ge).then_inc(routing_step, 1)
                dve.wait_ge(routing_step, done + 11)
                nc.vector.tensor_tensor(cand2[:], cand2[:], rank_sb[:], ALU.mult).then_inc(routing_step, 1)
                nc.vector.tensor_tensor(gsum[:], best1[:], best2[:], ALU.add).then_inc(routing_step, 1)
                dve.wait_ge(routing_step, done + 13)
                nc.vector.tensor_reduce(pick2[:], cand2[:], AX_X, ALU.max).then_inc(routing_step, 1)
                nc.vector.reciprocal(rgsum[:], gsum[:]).then_inc(routing_step, 1)
                dve.wait_ge(routing_step, done + 15)
                nc.vector.tensor_tensor(hot2[:], rank_sb[:], spread(pick2), ALU.is_equal).then_inc(routing_step, 1)
                dve.wait_ge(routing_step, done + 16)
                nc.vector.tensor_tensor(both[:], hot1[:], hot2[:], ALU.add).then_inc(routing_step, 1)
                dve.wait_ge(routing_step, done + 17)
                nc.vector.tensor_tensor(kept[:], prob[:], both[:], ALU.mult).then_inc(routing_step, 1)
                dve.wait_ge(routing_step, done + 18)
                dve.wait_ge(s_done, n)
                nc.vector.tensor_tensor(gates[:, :, 0:E], kept[:], spread(rgsum), ALU.mult).then_inc(gates_ready, 1)

            def step(n, last=False):
                split_h1(n)
                if not last:
                    split_y(n + 1)
                make_gates(n)
                if not last:
                    shift_logits(n + 1)

            nc.vector.memset(wc_sb[:], 0.0).then_inc(wc_zeroed, 1)
            nc.vector.memset(gates[:], 0.0).then_inc(zeroed, 1)
            nc.vector.memset(h2[:, 0, :], 0.0).then_inc(zeroed, 1)
            nc.vector.memset(wr_sb[:, :, E:], 0.0).then_inc(zeroed, 1)
            clamp_cond()
            nc.vector.memset(sT_sb[:, :, E:], 0.0)
            nc.vector.memset(x8[:], 0.0).then_inc(x8_zeroed, 1)
            split_w1()
            split_y(0)
            dve.wait_ge(consts_loaded, 16 * 3)
            shift_logits(0)
            split_w3()
            dve.wait_ge(s_zeroed, 1)
            step(0)
            with dve.Fori(1, NBLK - 1) as n:
                step(n)
            step(NBLK - 1, last=True)
            dve.wait_ge(s_done, NBLK)
            for k in range(KT):
                f = slice(k * P, (k + 1) * P)
                nc.vector.tensor_copy(s_sb[:, f], s_ps[:, f]).then_inc(s_copied, 1)
            dve.wait_ge(sT_done, 1)
            nc.vector.tensor_reduce(sT_sb[:, :, 0:E], quadrants(sT_ps), AX_X, ALU.add).then_inc(sT_copied, 1)
            dve.wait_ge(x8_loaded, 16 * KT)
            dve.wait_ge(o8_done, 1)
            nc.vector.tensor_tensor(o8[:], o8_ps[:, 0:P], x8[:], ALU.add).then_inc(o8_ready, 1)


def kernel(x, itok_B_1_198, L0_cond_weights, L0_ffn_w1, L0_ffn_w3, L0_ffn_w2, L0_ffn_wr):
    import concourse.bacc as bacc
    from concourse.bass_utils import run_bass_kernel_spmd

    experts = L0_ffn_wr.shape[0]
    ident = np.eye(P, dtype=np.float32)
    rank = np.tile(np.arange(experts, 0, -1, dtype=np.float32), (4, 1))
    arrays = {
        "x": np.ascontiguousarray(x),
        "cond": np.ascontiguousarray(itok_B_1_198),
        "cond_w": np.ascontiguousarray(L0_cond_weights),
        "w1T": np.ascontiguousarray(np.asarray(L0_ffn_w1).T),
        "w3T": np.ascontiguousarray(np.asarray(L0_ffn_w3).T),
        "w2T": np.ascontiguousarray(np.asarray(L0_ffn_w2).T),
        "wrT": np.ascontiguousarray(np.asarray(L0_ffn_wr).T),
        "ident": ident,
        "rank": rank,
    }
    nc = bacc.Bacc("TRN2", target_bir_lowering=False, num_devices=1)
    aps = {n: nc.dram_tensor(n, a.shape, mybir.dt.from_np(a.dtype), kind="ExternalInput").ap()
           for n, a in arrays.items()}
    out = nc.dram_tensor("out", x.shape, F32, kind="ExternalOutput").ap()
    adaln_ffn(nc, out=out, **aps)
    result = run_bass_kernel_spmd(nc, [arrays], core_ids=[0])
    return result.results[0]["out"]
```
